# Optimizing a Trainium2 kernel written in Bass

```python
import numpy as np
import jax
import jax.numpy as jnp

def _softmax(x, axis=-1):
    return jax.nn.softmax(x, axis=axis)

def _gelu(x):
    return jax.nn.gelu(x, approximate=True)

def _silu(x):
    return jax.nn.silu(x)

def _sigmoid(x):
    return jax.nn.sigmoid(x)

def _layernorm(x, axis=-1, eps=1e-05):
    m = jnp.mean(x, axis=axis, keepdims=True)
    v = jnp.var(x, axis=axis, keepdims=True)
    return (x - m) / jnp.sqrt(v + eps)

def _scatter_add(tgt, idx, src, axis=0):
    return tgt.at[idx].add(src)

def _segment_sum(src, seg, n):
    return jax.ops.segment_sum(src, seg, n)
kernel_name = 'mk_conv_seq_d1_conv_nchw256_r4_ba75cc'

def setup_inputs(seed: int=0):
    np.random.seed(seed)
    _w = jnp.asarray

    def _rec_inputs():
        import jax
        import jax.numpy as jnp
        _gk = jax.random.key(seed)
        x = -0.0002928 + 1 * jax.random.normal(jax.random.fold_in(_gk, 1), (4, 64, 16, 16), jnp.float32)
        return x
    x = _rec_inputs()

    def _L0_conv_setup():
        import jax, jax.numpy as jnp
        import numpy as np
        key = jax.random.key(seed)
        k1, k2, k3, k4 = jax.random.split(key, 4)
        b, c, h, w = (4, 64, 16, 16)
        dim_k = 64
        x = jax.random.normal(k1, (b, c, h, w), dtype=jnp.float32)
        limit = np.sqrt(6.0 / (dim_k + c)).astype(np.float32)
        W_q = jax.random.uniform(k2, (dim_k, c), minval=-limit, maxval=limit, dtype=jnp.float32)
        W_k = jax.random.uniform(k3, (dim_k, c), minval=-limit, maxval=limit, dtype=jnp.float32)
        W_v = jax.random.uniform(k4, (dim_k, c), minval=-limit, maxval=limit, dtype=jnp.float32)
        return {'x': x, 'W_q': W_q, 'W_k': W_k, 'W_v': W_v}
    _L0_conv_all = _L0_conv_setup()
    _L0_conv_in = {k: v for k, v in _L0_conv_all.items() if k in ('W_q', 'W_k', 'W_v')}
    del _L0_conv_all
    return {'x': x, 'L0_conv_W_q': _L0_conv_in['W_q'], 'L0_conv_W_k': _L0_conv_in['W_k'], 'L0_conv_W_v': _L0_conv_in['W_v']}

def reference(x, L0_conv_W_q, L0_conv_W_k, L0_conv_W_v):
    import jax
    import jax.numpy as jnp

    def _L0_conv_ref(x, W_q, W_k, W_v):
        import jax, jax.numpy as jnp
        import numpy as np
        b, c, h, w = x.shape
        dim_k = W_q.shape[0]
        xt = x.reshape(b, c, h * w)
        Q = jnp.einsum('kc,bcn->bnk', W_q, xt)
        K = jnp.einsum('kc,bcn->bkn', W_k, xt)
        V = jnp.einsum('kc,bcn->bnk', W_v, xt)
        scores = jnp.einsum('bnk,bkm->bnm', Q, K) / jnp.sqrt(jnp.float32(dim_k))
        A = jax.nn.softmax(scores, axis=2)
        out = jnp.einsum('bnm,bmk->bnk', A, V)
        out = out.transpose(0, 2, 1).reshape(b, dim_k, h, w)
        return x + out

    def _gn(v, G=32, eps=1e-05):
        B_, C_, H_, W_ = v.shape
        g = v.reshape(B_, G, C_ // G, H_, W_)
        m = jnp.mean(g, axis=(2, 3, 4), keepdims=True)
        s = jnp.var(g, axis=(2, 3, 4), keepdims=True)
        return ((g - m) / jnp.sqrt(s + eps)).reshape(v.shape)

    def _ln_c(v, eps=1e-06):
        m = jnp.mean(v, axis=1, keepdims=True)
        s = jnp.var(v, axis=1, keepdims=True)
        return (v - m) / jnp.sqrt(s + eps)

    def _ln_t(v, eps=1e-05):
        m = jnp.mean(v, axis=-1, keepdims=True)
        s = jnp.var(v, axis=-1, keepdims=True)
        return (v - m) / jnp.sqrt(s + eps)

    def _to_tokens(v):
        B_, C_, H_, W_ = v.shape
        return v.reshape(B_, C_, H_ * W_).transpose(0, 2, 1)

    def _from_tokens(t, like):
        B_, C_, H_, W_ = like.shape
        return t.transpose(0, 2, 1).reshape(B_, C_, H_, W_)
    x = _L0_conv_ref(x, L0_conv_W_q, L0_conv_W_k, L0_conv_W_v)
    return x

_drawn_inputs = setup_inputs


def setup_inputs(seed=0):
    import zlib

    import numpy as np

    out = dict(_drawn_inputs(seed))
    spreads = {}
    factors = {}
    for name, (base, spread) in spreads.items():
        noise = np.random.default_rng([zlib.crc32(name.encode()), seed]).standard_normal(out[name].shape)
        drawn = base * np.exp(spread * noise) if base else spread * noise
        out[name] = jnp.asarray(drawn.astype(out[name].dtype))
    for name, factor in factors.items():
        out[name] = (out[name] * factor).astype(out[name].dtype)
    return out
```

```python
from contextlib import ExitStack

import concourse.bass as bass
from concourse import mybir

F32 = mybir.dt.float32
ALU = mybir.AluOpType
ACT = mybir.ActivationFunctionType
AX = mybir.AxisListType

P = 128
C = 64
D = 64
B = 4
N = 256
PAIRS = B // 2
CHUNKS = N // P
WARM = 24


def attention_program(nc: bass.Bass, x: bass.AP, w_qqk: bass.AP, w_v2: bass.AP, out: bass.AP):
    with ExitStack() as ctx:
        def sb(name, shape):
            return ctx.enter_context(nc.sbuf_tensor(name, shape, F32))

        def bank(name):
            return ctx.enter_context(nc.psum_tensor(name, [P, 512], F32))

        def sem(name):
            return ctx.enter_context(nc.semaphore(name))

        x_sb = sb("x_sb", [P, PAIRS, N])
        qqk_sb = sb("qqk_sb", [D, 3 * C])
        wv2_sb = sb("wv2_sb", [P, P])
        m2_sb = sb("m2_sb", [P, P])
        z_sb = sb("z_sb", [P, PAIRS, N])
        v_sb = sb("v_sb", [P, PAIRS, CHUNKS, P])
        ident = sb("ident", [P, P])
        zeros = sb("zeros", [P, 512])
        low = sb("low", [P, B, CHUNKS])
        total = sb("total", [P, B, CHUNKS])
        inverse = sb("inverse", [P, B, CHUNKS])
        e_sb = sb("e_sb", [P, B, CHUNKS, N])
        a_sb = sb("a_sb", [P, B, CHUNKS, N])
        at_sb = sb("at_sb", [P, B, CHUNKS, N])
        y_sb = sb("y_sb", [P, PAIRS, N])
        scratch = sb("scratch", [P, 1])

        banks = [bank(f"bank{i}") for i in range(8)]
        s_ps = banks[0:4]
        z_ps = banks[4:6]
        v_ps, m_ps = banks[6], banks[7]
        at_ps = [banks[4], banks[5], banks[6], banks[7]]
        o_ps = [banks[0], banks[2]]

        qqk_in = sem("qqk_in")
        wv_in = sem("wv_in")
        x_in = [sem(f"x_in{p}") for p in range(PAIRS)]
        zeroed = sem("zeroed")
        m2_zeroed = sem("m2_zeroed")
        ident_zeroed = sem("ident_zeroed")
        ident_ready = sem("ident_ready")
        m_ready = sem("m_ready")
        m2_ready = sem("m2_ready")
        z_ready = sem("z_ready")
        z_copied = [sem(f"z_copied{p}") for p in range(PAIRS)]
        v_ready = sem("v_ready")
        v_copied = sem("v_copied")
        scores_ready = sem("scores_ready")
        low_ready = sem("low_ready")
        exp_ready = sem("exp_ready")
        inverse_ready = sem("inverse_ready")
        softmax_ready = sem("softmax_ready")
        transposed = sem("transposed")
        at_copied = [sem(f"at_copied{b}") for b in range(B)]
        o_ready = sem("o_ready")
        y_ready = sem("y_ready")
        stored = sem("stored")

        x_pairs = x.rearrange("(p r) n -> p r n", p=PAIRS)
        out_pairs = out.rearrange("(p r) n -> p r n", p=PAIRS)

        block = ctx.enter_context(nc.Block())

        @block.sync
        def _(sp):
            sp.dma_start(qqk_sb[:], w_qqk).then_inc(qqk_in, 16)
            sp.dma_start(x_sb[:, 1, :], x_pairs[1]).then_inc(x_in[1], 16)
            for p in range(PAIRS):
                sp.wait_ge(y_ready, p + 1)
                sp.dma_start(out_pairs[p], y_sb[:, p, :]).then_inc(stored, 16)
            sp.wait_ge(stored, 16 * PAIRS)

        @block.gpsimd
        def _(pool):
            nc.gpsimd.memset(ident[:], 0.0).then_inc(ident_zeroed, 1)
            pool.wait_ge(ident_zeroed, 1)
            nc.gpsimd.affine_select(out=ident[:], in_=ident[:], compare_op=ALU.not_equal, fill=1.0,
                                    base=0, pattern=[[-1, P]], channel_multiplier=1).then_inc(ident_ready, 1)
            for b in range(B):
                pool.wait_ge(inverse_ready, b + 1)
                for c in range(CHUNKS):
                    nc.gpsimd.tensor_scalar(a_sb[:, b, c, :], e_sb[:, b, c, :], inverse[:, b, c:c + 1], 1.0,
                                            ALU.mult, ALU.mult).then_inc(softmax_ready, 1)

        @block.scalar
        def _(act):
            act.dma_start(x_sb[:, 0, :], x_pairs[0]).then_inc(x_in[0], 16)
            act.dma_start(wv2_sb[:], w_v2).then_inc(wv_in, 16)
            act.wait_ge(zeroed, 1)
            nc.scalar.activation(scratch[:], zeros[:, 0:1], ACT.Exp)
            act.wait_ge(z_ready, 2)
            nc.scalar.copy(z_sb[:, 1, :], z_ps[1][:, 0:N]).then_inc(z_copied[1], 1)

            def exponentials(b):
                act.wait_ge(low_ready, b + 1)
                for c in range(CHUNKS):
                    nc.scalar.activation(e_sb[:, b, c, :], s_ps[b][:, c * N:(c + 1) * N], ACT.Exp,
                                         bias=low[:, b, c:c + 1], scale=-1.0,
                                         accum_out=total[:, b, c:c + 1]).then_inc(exp_ready, 1)

            def copy_transposed(b):
                act.wait_ge(transposed, b + 1)
                nc.scalar.copy(at_sb[:, b, :, :].rearrange("p c n -> p (c n)"), at_ps[b][:]).then_inc(at_copied[b], 1)

            exponentials(0)
            exponentials(1)
            exponentials(2)
            exponentials(3)
            copy_transposed(3)

        @block.vector
        def _(dve):
            nc.vector.memset(zeros[:], 0.0).then_inc(zeroed, 1)
            nc.vector.memset(m2_sb[:], 0.0).then_inc(m2_zeroed, 1)
            dve.wait_ge(m2_zeroed, 1)
            dve.wait_ge(m_ready, 1)
            for h in range(2):
                rows = slice(h * C, (h + 1) * C)
                nc.vector.tensor_scalar(m2_sb[rows, rows], m_ps[rows, 0:C], -float(D) ** -0.5, None,
                                        ALU.mult).then_inc(m2_ready, 1)
            dve.wait_ge(z_ready, 1)
            nc.vector.tensor_copy(z_sb[:, 0, :], z_ps[0][:, 0:N]).then_inc(z_copied[0], 1)

            def least(b):
                dve.wait_ge(scores_ready, b + 1)
                nc.vector.tensor_reduce(low[:, b, :], s_ps[b][:].rearrange("p (c n) -> p c n", c=CHUNKS),
                                        AX.X, ALU.min).then_inc(low_ready, 1)

            def invert(b):
                dve.wait_ge(exp_ready, CHUNKS * (b + 1))
                nc.vector.reciprocal(inverse[:, b, :], total[:, b, :]).then_inc(inverse_ready, 1)

            def copy_transposed(b):
                dve.wait_ge(transposed, b + 1)
                nc.vector.tensor_copy(at_sb[:, b, :, :].rearrange("p c n -> p (c n)"), at_ps[b][:]).then_inc(at_copied[b], 1)

            def add_input(p):
                dve.wait_ge(o_ready, p + 1)
                nc.vector.tensor_tensor(y_sb[:, p, :], o_ps[p][:, 0:N], x_sb[:, p, :], ALU.add).then_inc(y_ready, 1)

            least(0)
            least(1)
            dve.wait_ge(v_ready, 1)
            nc.vector.tensor_copy(v_sb[:].rearrange("p a c k -> p (a c k)"), v_ps[:]).then_inc(v_copied, 1)
            invert(0)
            least(2)
            invert(1)
            copy_transposed(0)
            least(3)
            invert(2)
            copy_transposed(1)
            invert(3)
            add_input(0)
            copy_transposed(2)
            add_input(1)

        @block.tensor
        def _(pe):
            pe.wait_ge(zeroed, 1)
            for _ in range(WARM):
                nc.tensor.matmul(banks[7][:, 0:P], zeros[:, 0:P].bitcast(mybir.dt.bfloat16)[:, 0:P],
                                 zeros[:].bitcast(mybir.dt.bfloat16)[:, 0:P], start=True, stop=True)
            pe.wait_ge(qqk_in, 16)
            nc.tensor.matmul(m_ps[:, 0:C], qqk_sb[:, 0:2 * C], qqk_sb[:, 2 * C:3 * C],
                             start=True, stop=True).then_inc(m_ready, 1)

            def values(p):
                pe.wait_ge(x_in[p], 16)
                for c in range(CHUNKS):
                    at = (p * CHUNKS + c) * P
                    last = nc.tensor.matmul(v_ps[:, at:at + P], x_sb[:, p, c * P:(c + 1) * P], wv2_sb[:],
                                            start=True, stop=True)
                return last

            def left_side(p):
                pe.wait_ge(x_in[p], 16)
                nc.tensor.matmul(z_ps[p][:, 0:N], m2_sb[:], x_sb[:, p, :], start=True, stop=True).then_inc(z_ready, 1)

            def scores(p):
                pe.wait_ge(z_copied[p], 1)
                for c in range(CHUNKS):
                    for h in range(2):
                        rows = slice(h * C, (h + 1) * C)
                        mm = nc.tensor.matmul(s_ps[2 * p + h][:, c * N:(c + 1) * N], z_sb[rows, p, c * P:(c + 1) * P],
                                              x_sb[rows, p, :], start=True, stop=True)
                        if c == CHUNKS - 1:
                            mm.then_inc(scores_ready, 1)

            def transpose(b):
                if b == 2:
                    pe.wait_ge(v_copied, 1)
                for c in range(CHUNKS):
                    pe.wait_ge(softmax_ready, CHUNKS * b + c + 1)
                    for k in range(CHUNKS):
                        mm = nc.tensor.transpose(at_ps[b][:, k * N + c * P:k * N + (c + 1) * P],
                                                 a_sb[:, b, c, k * P:(k + 1) * P], ident[:])
                mm.then_inc(transposed, 1)

            def weighted_values(p):
                if p == 0:
                    pe.wait_ge(v_copied, 1)
                for h in range(2):
                    pe.wait_ge(at_copied[2 * p + h], 1)
                for k in range(CHUNKS):
                    for h in range(2):
                        mm = nc.tensor.matmul(o_ps[p][h * D:(h + 1) * D, 0:N], v_sb[:, p, k, h * D:(h + 1) * D],
                                              at_sb[:, 2 * p + h, k, :], start=(k == 0), stop=(k == CHUNKS - 1))
                mm.then_inc(o_ready, 1)

            pe.wait_ge(m2_ready, 2)
            left_side(0)
            pe.wait_ge(wv_in, 16)
            values(0)
            left_side(1)
            scores(0)
            values(1).then_inc(v_ready, 1)
            scores(1)
            pe.wait_ge(ident_ready, 1)
            transpose(0)
            transpose(1)
            weighted_values(0)
            transpose(2)
            transpose(3)
            weighted_values(1)


def kernel(x, L0_conv_W_q, L0_conv_W_k, L0_conv_W_v):
    import numpy as np
    import concourse.bacc as bacc
    from concourse.bass_utils import run_bass_kernel_spmd

    shape = x.shape
    w_q, w_k, w_v = (np.asarray(w) for w in (L0_conv_W_q, L0_conv_W_k, L0_conv_W_v))
    w_v2 = np.zeros((P, P), np.float32)
    w_v2[0:C, 0:D] = w_v.T
    w_v2[C:P, D:P] = w_v.T
    arrays = {
        "x_dram": np.ascontiguousarray(np.asarray(x).reshape(B * C, N)),
        "w_qqk_dram": np.ascontiguousarray(np.concatenate([w_q, w_q, w_k], axis=1)),
        "w_v2_dram": w_v2,
    }
    nc = bacc.Bacc("TRN2", target_bir_lowering=False, num_devices=1)
    ins = [nc.dram_tensor(name, a.shape, F32, kind="ExternalInput").ap() for name, a in arrays.items()]
    out = nc.dram_tensor("out_dram", (B * D, N), F32, kind="ExternalOutput").ap()
    attention_program(nc, *ins, out)
    result = run_bass_kernel_spmd(nc, [arrays], core_ids=[0])
    return result.results[0]["out_dram"].reshape(shape)
```

```python
from contextlib import ExitStack

import concourse.bass as bass
from concourse import mybir

F32 = mybir.dt.float32
BF16 = mybir.dt.bfloat16
ALU = mybir.AluOpType
ACT = mybir.ActivationFunctionType
AX = mybir.AxisListType

P = 128
C = 64
D = 64
B = 4
N = 256
BANK = 512
HALVES = 2
PAIRS = B // HALVES
CHUNKS = N // P

TILES = [(p, c, h) for p in range(PAIRS) for c in range(CHUNKS) for h in range(HALVES)]
PAIR_TILES = CHUNKS * HALVES
T = len(TILES)

WARM_LOADS = 24
WARM_PRODUCT = 2


def attention_program(nc: bass.Bass, x: bass.AP, w_qk: bass.AP, w_v2: bass.AP, out: bass.AP):
    with ExitStack() as ctx:
        def sb(name, shape):
            return ctx.enter_context(nc.sbuf_tensor(name, shape, F32))

        def sem(name):
            return ctx.enter_context(nc.semaphore(name))

        x_sb = sb("x_sb", [P, PAIRS, N])
        qk_sb = sb("qk_sb", [D, 4 * C])
        wv2_sb = sb("wv2_sb", [P, P])
        m2_sb = sb("m2_sb", [P, P])
        z_sb = sb("z_sb", [P, PAIRS, N])
        v_sb = sb("v_sb", [P, PAIRS, CHUNKS, P])
        ident = sb("ident", [P, P])
        low = sb("low", [P, T])
        total = sb("total", [P, T])
        inverse = sb("inverse", [P, T])
        e_sb = sb("e_sb", [P, T, N])
        a_sb = sb("a_sb", [P, T, N])
        at_sb = sb("at_sb", [P, PAIRS, HALVES, CHUNKS, N])
        y_sb = sb("y_sb", [P, PAIRS, N])
        table_out = sb("table_out", [P, 1])
        ones = nc.const_aps.tensor(1.0, [P, P], BF16)

        banks = [ctx.enter_context(nc.psum_tensor(f"bank{i}", [P, BANK], F32)) for i in range(8)]
        s_ps = [banks[t % 4][:, 0:N] for t in range(T)]
        z_ps = [banks[4][:, 0:N], banks[5][:, 0:N]]
        m_ps = banks[7][:, 0:P]
        v_ps = banks[6][:]
        at_ps = [banks[(4, 5, 7, 6)[t % 4]][:, 0:N] for t in range(T)]
        o_ps = {(0, 0): banks[0][:, 0:N], (1, 0): banks[1][:, 0:P], (1, 1): banks[2][:, 0:P]}

        qk_in = sem("qk_in")
        wv_in = sem("wv_in")
        x_in = [sem(f"x_in{p}") for p in range(PAIRS)]
        m2_zeroed = sem("m2_zeroed")
        ident_zeroed = sem("ident_zeroed")
        ident_ready = sem("ident_ready")
        m_ready = sem("m_ready")
        m2_copied = [sem(f"m2_copied{h}") for h in range(HALVES)]
        z_ready = sem("z_ready")
        z_copied = [sem(f"z_copied{p}") for p in range(PAIRS)]
        v_ready = sem("v_ready")
        v_copied = sem("v_copied")
        scores_ready = sem("scores_ready")
        low_ready = sem("low_ready")
        exp_ready = sem("exp_ready")
        inverse_ready = sem("inverse_ready")
        softmax_ready = sem("softmax_ready")
        transposed = sem("transposed")
        at_copied = [sem(f"at_copied{t}") for t in range(T)]
        o_ready = sem("o_ready")
        y_ready = sem("y_ready")
        stored = sem("stored")

        x_pairs = x.rearrange("(p r) n -> p r n", p=PAIRS)
        out_pairs = out.rearrange("(p r) n -> p r n", p=PAIRS)

        def half(h):
            return slice(h * C, (h + 1) * C)

        def chunk(c):
            return slice(c * P, (c + 1) * P)

        def transposed_in_sbuf(t):
            p, c, h = TILES[t]
            return at_sb[:, p, h, :, chunk(c)]

        def transposed_in_psum(t):
            return at_ps[t].rearrange("r (k n) -> r k n", k=CHUNKS)

        block = ctx.enter_context(nc.Block())

        @block.sync
        def _(sp):
            sp.dma_start(qk_sb[:], w_qk).then_inc(qk_in, 16)
            sp.dma_start(x_sb[:, 1, :], x_pairs[1]).then_inc(x_in[1], 16)
            sp.wait_ge(y_ready, 1)
            sp.dma_start(out_pairs[0], y_sb[:, 0, :]).then_inc(stored, 16)
            for c in range(CHUNKS):
                sp.wait_ge(y_ready, 2 + c)
                sp.dma_start(out_pairs[1][:, chunk(c)], y_sb[:, 1, chunk(c)]).then_inc(stored, 16)
            sp.wait_ge(stored, 16 * (1 + CHUNKS))

        @block.gpsimd
        def _(pool):
            pool.dma_start(wv2_sb[:], w_v2).then_inc(wv_in, 16)
            nc.gpsimd.memset(m2_sb[:], 0.0).then_inc(m2_zeroed, 1)
            nc.gpsimd.memset(ident[:], 0.0).then_inc(ident_zeroed, 1)
            pool.wait_ge(ident_zeroed, 1)
            nc.gpsimd.affine_select(out=ident[:], in_=ident[:], compare_op=ALU.not_equal, fill=1.0,
                                    base=0, pattern=[[-1, P]], channel_multiplier=1).then_inc(ident_ready, 1)
            for t in range(T):
                pool.wait_ge(inverse_ready, t + 1)
                nc.gpsimd.tensor_scalar(a_sb[:, t, :], e_sb[:, t, :], inverse[:, t:t + 1], 1.0,
                                        ALU.mult, ALU.mult).then_inc(softmax_ready, 1)

        @block.scalar
        def _(act):
            def exponentials(t):
                act.wait_ge(low_ready, t + 1)
                nc.scalar.activation(e_sb[:, t, :], s_ps[t], ACT.Exp, bias=low[:, t:t + 1], scale=-1.0,
                                     accum_out=total[:, t:t + 1]).then_inc(exp_ready, 1)

            def copy_transposed(t):
                act.wait_ge(transposed, t + 1)
                nc.scalar.copy(transposed_in_sbuf(t), transposed_in_psum(t)).then_inc(at_copied[t], 1)

            act.dma_start(x_sb[:, 0, :], x_pairs[0]).then_inc(x_in[0], 16)
            nc.scalar.activation(table_out[:], ones[:, 0:1], ACT.Exp)
            act.wait_ge(m2_zeroed, 1)
            act.wait_ge(m_ready, 1)
            nc.scalar.mul(m2_sb[half(0), half(0)], m_ps[half(0), half(0)], -float(D) ** -0.5).then_inc(m2_copied[0], 1)
            act.wait_ge(z_ready, 1)
            nc.scalar.copy(z_sb[:, 0, :], z_ps[0]).then_inc(z_copied[0], 1)
            for t in range(0, 6):
                exponentials(t)
            for t in (0, 2, 1):
                copy_transposed(t)
            for t in (6, 7):
                exponentials(t)
            for t in (4, 6):
                copy_transposed(t)

        @block.vector
        def _(dve):
            def least(t):
                dve.wait_ge(scores_ready, t + 1)
                nc.vector.tensor_reduce(low[:, t:t + 1], s_ps[t], AX.X, ALU.min).then_inc(low_ready, 1)

            def invert(t):
                dve.wait_ge(exp_ready, t + 1)
                nc.vector.reciprocal(inverse[:, t:t + 1], total[:, t:t + 1]).then_inc(inverse_ready, 1)

            def copy_transposed(t):
                dve.wait_ge(transposed, t + 1)
                nc.vector.tensor_copy(transposed_in_sbuf(t), transposed_in_psum(t)).then_inc(at_copied[t], 1)

            def add_input(part, p, cols, weighted):
                dve.wait_ge(o_ready, part + 1)
                nc.vector.tensor_tensor(y_sb[:, p, cols], weighted, x_sb[:, p, cols], ALU.add).then_inc(y_ready, 1)

            dve.wait_ge(m2_zeroed, 1)
            dve.wait_ge(m_ready, 1)
            nc.vector.tensor_scalar(m2_sb[half(1), half(1)], m_ps[half(1), half(1)], -float(D) ** -0.5, None,
                                    ALU.mult).then_inc(m2_copied[1], 1)
            dve.wait_ge(z_ready, 2)
            nc.vector.tensor_copy(z_sb[:, 1, :], z_ps[1]).then_inc(z_copied[1], 1)

            least(0)
            least(1)
            for t in range(4):
                least(t + 2)
                invert(t)
            invert(4)
            dve.wait_ge(v_ready, PAIRS * CHUNKS)
            nc.vector.tensor_copy(v_sb[:].rearrange("r p c k -> r (p c k)"), v_ps).then_inc(v_copied, 1)
            invert(5)
            least(6)
            least(7)
            copy_transposed(3)
            invert(6)
            invert(7)
            copy_transposed(5)
            add_input(0, 0, slice(0, N), o_ps[0, 0])
            copy_transposed(7)
            add_input(1, 1, chunk(0), o_ps[1, 0])
            add_input(2, 1, chunk(1), o_ps[1, 1])

        @block.tensor
        def _(pe):
            def idle_matmuls(count):
                for _ in range(count):
                    nc.tensor.matmul(s_ps[0][:, 0:P], ones, ones, start=True, stop=True)

            def values(p, c):
                pe.wait_ge(x_in[p], 16)
                pe.wait_ge(wv_in, 16)
                nc.tensor.matmul(v_ps[:, chunk(p * CHUNKS + c)], x_sb[:, p, chunk(c)], wv2_sb[:],
                                 start=True, stop=True).then_inc(v_ready, 1)

            def left_side(p):
                pe.wait_ge(x_in[p], 16)
                for h in range(HALVES):
                    pe.wait_ge(m2_copied[h], 1)
                nc.tensor.matmul(z_ps[p], m2_sb[:], x_sb[:, p, :], start=True, stop=True).then_inc(z_ready, 1)

            def scores(t):
                p, c, h = TILES[t]
                pe.wait_ge(z_copied[p], 1)
                if t >= 4:
                    pe.wait_ge(exp_ready, t - 3)
                nc.tensor.matmul(s_ps[t], z_sb[half(h), p, chunk(c)], x_sb[half(h), p, :],
                                 start=True, stop=True).then_inc(scores_ready, 1)

            def transpose(t):
                if t in (0, 1):
                    pe.wait_ge(z_copied[t], 1)
                elif t == 2:
                    for h in range(HALVES):
                        pe.wait_ge(m2_copied[h], 1)
                elif t == 3:
                    pe.wait_ge(v_copied, 1)
                else:
                    pe.wait_ge(at_copied[t - 4], 1)
                pe.wait_ge(softmax_ready, t + 1)
                for k in range(CHUNKS):
                    last = nc.tensor.transpose(at_ps[t][:, chunk(k)], a_sb[:, t, chunk(k)], ident[:])
                last.then_inc(transposed, 1)

            def weighted_values(p, cols, weighted):
                for k in range(CHUNKS):
                    for h in range(HALVES):
                        last = nc.tensor.matmul(weighted[half(h), :], v_sb[:, p, k, half(h)], at_sb[:, p, h, k, cols],
                                                start=(k == 0), stop=(k == CHUNKS - 1))
                last.then_inc(o_ready, 1)

            idle_matmuls(WARM_LOADS)
            pe.wait_ge(qk_in, 16)
            nc.tensor.matmul(m_ps, qk_sb[:, 0:2 * C], qk_sb[:, 2 * C:4 * C], start=True, stop=True).then_inc(m_ready, 1)
            idle_matmuls(WARM_PRODUCT)

            values(0, 0)
            values(0, 1)
            left_side(0)
            values(1, 0)
            left_side(1)
            for t in range(0, 6):
                scores(t)
            values(1, 1)
            scores(6)
            pe.wait_ge(ident_ready, 1)
            for t in (0, 1, 2):
                transpose(t)
            scores(7)
            for t in (3, 4, 5):
                transpose(t)
            pe.wait_ge(v_copied, 1)
            pe.wait_ge(exp_ready, 5)
            for t in range(PAIR_TILES):
                pe.wait_ge(at_copied[t], 1)
            weighted_values(0, slice(0, N), o_ps[0, 0])
            transpose(6)
            transpose(7)
            for c in range(CHUNKS):
                pe.wait_ge(exp_ready, 6 + c)
                for h in range(HALVES):
                    pe.wait_ge(at_copied[PAIR_TILES + c * HALVES + h], 1)
                weighted_values(1, chunk(c), o_ps[1, c])


def kernel(x, L0_conv_W_q, L0_conv_W_k, L0_conv_W_v):
    import numpy as np
    import concourse.bacc as bacc
    from concourse.bass_utils import run_bass_kernel_spmd

    shape = x.shape
    w_q, w_k, w_v = (np.asarray(w) for w in (L0_conv_W_q, L0_conv_W_k, L0_conv_W_v))
    w_v2 = np.zeros((P, P), np.float32)
    w_v2[0:C, 0:D] = w_v.T
    w_v2[C:P, D:P] = w_v.T
    arrays = {
        "x_dram": np.ascontiguousarray(np.asarray(x).reshape(B * C, N)),
        "w_qk_dram": np.ascontiguousarray(np.concatenate([w_q, w_q, w_k, w_k], axis=1)),
        "w_v2_dram": w_v2,
    }
    nc = bacc.Bacc("TRN2", target_bir_lowering=False, num_devices=1)
    ins = [nc.dram_tensor(name, a.shape, F32, kind="ExternalInput").ap() for name, a in arrays.items()]
    out = nc.dram_tensor("out_dram", (B * D, N), F32, kind="ExternalOutput").ap()
    attention_program(nc, *ins, out)
    result = run_bass_kernel_spmd(nc, [arrays], core_ids=[0])
    return result.results[0]["out_dram"].reshape(shape)
```
